# Optimizing a Trainium2 kernel written in Bass

```python
import numpy as np
import jax
import jax.numpy as jnp

def _softmax(x, axis=-1):
    return jax.nn.softmax(x, axis=axis)
def _gelu(x):
    return jax.nn.gelu(x, approximate=True)
def _silu(x):
    return jax.nn.silu(x)
def _sigmoid(x):
    return jax.nn.sigmoid(x)
def _layernorm(x, axis=-1, eps=1e-5):
    m = jnp.mean(x, axis=axis, keepdims=True)
    v = jnp.var(x, axis=axis, keepdims=True)
    return (x - m) / jnp.sqrt(v + eps)
def _scatter_add(tgt, idx, src, axis=0):
    return tgt.at[idx].add(src)
def _segment_sum(src, seg, n):
    return jax.ops.segment_sum(src, seg, n)

kernel_name = 'mk_conv_preact_d1_conv_nchw512_05ad7e'

def setup_inputs(seed: int = 0):
    np.random.seed(seed)
    _w = jnp.asarray
    def _rec_inputs():
        import jax
        import jax.numpy as jnp
        _gk = jax.random.key(seed)
        x = -8.268e-05 + 0.9999 * jax.random.normal(jax.random.fold_in(_gk, 1), (32, 512, 56, 56), jnp.float32)
        return x
    x = _rec_inputs()
    def _L0_conv_setup():
        import jax, jax.numpy as jnp
        import numpy as np
        IN_C = 512
        OUT_C = 512
        S = 1
        EPS = 1e-05
        key = jax.random.key(seed)
        k1, k2 = jax.random.split(key)
        x = jax.random.normal(k1, (32, IN_C, 56, 56), dtype=jnp.float32)
        conv = jax.random.normal(k2, (IN_C + (OUT_C - 1) * S, 1, 1), dtype=jnp.float32)
        gamma = jnp.ones((OUT_C,), dtype=jnp.float32)
        beta = jnp.zeros((OUT_C,), dtype=jnp.float32)
        return {'x': x, 'conv': conv, 'gamma': gamma, 'beta': beta}
    _L0_conv_all = _L0_conv_setup()
    _L0_conv_in = {k: v for k, v in _L0_conv_all.items() if k in ('conv', 'gamma', 'beta', )}
    del _L0_conv_all

    return {
        "x": x,
        "L0_conv_conv": _L0_conv_in["conv"],
        "L0_conv_gamma": _L0_conv_in["gamma"],
        "L0_conv_beta": _L0_conv_in["beta"],
    }

def reference(x, L0_conv_conv, L0_conv_gamma, L0_conv_beta):
    import jax
    import jax.numpy as jnp
    def _L0_conv_ref(x, conv, gamma, beta):
        import jax, jax.numpy as jnp
        import numpy as np
        IN_C = 512
        OUT_C = 512
        S = 1
        EPS = 1e-05
        idx = jnp.arange(IN_C)[None, :] + S * jnp.arange(OUT_C)[:, None]
        kernel = conv[:, 0, 0][idx]
        out = jnp.einsum('bchw,oc->bohw', x, kernel)
        mean = jnp.mean(out, axis=(0, 2, 3), keepdims=True)
        var = jnp.var(out, axis=(0, 2, 3), keepdims=True)
        out = (out - mean) * jax.lax.rsqrt(var + EPS)
        out = out * gamma[None, :, None, None] + beta[None, :, None, None]
        return jax.nn.relu(out)

    def _gn(v, G=32, eps=1e-5):
        B_, C_, H_, W_ = v.shape
        g = v.reshape(B_, G, C_ // G, H_, W_)
        m = jnp.mean(g, axis=(2, 3, 4), keepdims=True)
        s = jnp.var(g, axis=(2, 3, 4), keepdims=True)
        return ((g - m) / jnp.sqrt(s + eps)).reshape(v.shape)

    def _ln_c(v, eps=1e-6):
        m = jnp.mean(v, axis=1, keepdims=True)
        s = jnp.var(v, axis=1, keepdims=True)
        return (v - m) / jnp.sqrt(s + eps)

    def _ln_t(v, eps=1e-5):
        m = jnp.mean(v, axis=-1, keepdims=True)
        s = jnp.var(v, axis=-1, keepdims=True)
        return (v - m) / jnp.sqrt(s + eps)

    def _to_tokens(v):
        B_, C_, H_, W_ = v.shape
        return v.reshape(B_, C_, H_ * W_).transpose(0, 2, 1)
    def _from_tokens(t, like):
        B_, C_, H_, W_ = like.shape
        return t.transpose(0, 2, 1).reshape(B_, C_, H_, W_)

    x = x + _L0_conv_ref(_gn(x), L0_conv_conv, L0_conv_gamma, L0_conv_beta)
    return x


_drawn_inputs = setup_inputs


def setup_inputs(seed=0):
    import zlib

    import numpy as np

    out = dict(_drawn_inputs(seed))
    spreads = {'L0_conv_gamma': (1.0, 0.2), 'L0_conv_beta': (0.0, 0.1)}
    factors = {}
    for name, (base, spread) in spreads.items():
        noise = np.random.default_rng([zlib.crc32(name.encode()), seed]).standard_normal(out[name].shape)
        drawn = base * np.exp(spread * noise) if base else spread * noise
        out[name] = jnp.asarray(drawn.astype(out[name].dtype))
    for name, factor in factors.items():
        out[name] = (out[name] * factor).astype(out[name].dtype)
    return out
```

```python
from contextlib import ExitStack

import numpy as np
import concourse.bass as bass
from concourse import mybir

F32 = mybir.dt.float32
F16 = mybir.dt.float16
ALU = mybir.AluOpType
ACT = mybir.ActivationFunctionType
AX_X = mybir.AxisListType.X

P = 128
GROUPS = 32
GN_EPS = 1e-5
BN_EPS = 1e-5
G_SCALE = 64.0
W_MAX = 1024.0


def conv_block_kernel(nc, x, conv, gamma, beta, group_avg, out):
    B, C, S = x.shape
    CT = C // P
    NCH = 7
    N = S // NCH
    PAIRS = B // 2
    U = 2 * NCH
    WCOLS = (2 * CT - 1) * P
    NBANK = 7
    TAPS = conv.shape[0]

    x_v = x.rearrange("b (t p) s -> b p t s", p=P)
    out_v = out.rearrange("b (t p) s -> b p t s", p=P)
    y_scratch = nc.dram_tensor("y_scratch", (B, C, S), F32, kind="Internal").ap()
    y_v = y_scratch.rearrange("b (t p) s -> b p t s", p=P)
    hankel_src = bass.AP(conv.tensor, 0, [[1, P], [1, WCOLS]])
    conv_rows = bass.AP(conv.tensor, 0, [[0, P], [1, TAPS]])

    with ExitStack() as ctx:
        def sb(name, shape, dt=F32):
            return ctx.enter_context(nc.sbuf_tensor(name, shape, dt))

        def sem(name):
            return ctx.enter_context(nc.semaphore(name))

        xbuf = sb("xbuf", [P, 2, CT, S])
        split = sb("split", [P, 2, 2, CT, N], F16)
        y_sb = sb("y_sb", [P, 2, CT, N])
        hankel = sb("hankel", [P, WCOLS])
        taps = sb("taps", [P, TAPS])
        w_hi = sb("w_hi", [P, WCOLS], F16)
        w_lo = sb("w_lo", [P, WCOLS], F16)
        gavg = sb("gavg", [P, P])
        gam = sb("gam", [P, CT])
        bet = sb("bet", [P, CT])
        w_scale = sb("w_scale", [P, 4])
        x_stats = sb("x_stats", [P, CT, NCH, 6])
        x_mv = sb("x_mv", [P, CT, 2])
        g_mean = sb("g_mean", [P, CT])
        dev = sb("dev", [P, CT])
        dev2 = sb("dev2", [P, CT])
        g_e = sb("g_e", [P, CT])
        g_var = sb("g_var", [P, CT])
        g_std = sb("g_std", [P, CT])
        g_r = sb("g_r", [P, CT])
        g_t = sb("g_t", [P, CT])
        coef = sb("coef", [P, 2, 2, CT])
        y_stats = sb("y_stats", [P, CT, NCH, 6])
        y_mv = sb("y_mv", [P, CT, B, 2])
        y_mv1 = sb("y_mv1", [P, CT, 2])
        fence = sb("fence", [P, 1])
        m_stats = sb("m_stats", [P, CT, 6])
        m_mv = sb("m_mv", [P, CT, 2])
        v_sum = sb("v_sum", [P, CT])
        b_var = sb("b_var", [P, CT])
        b_std = sb("b_std", [P, CT])
        b_r = sb("b_r", [P, CT])
        b_t = sb("b_t", [P, CT])
        bn_a = sb("bn_a", [P, CT])
        bn_b = sb("bn_b", [P, CT])
        banks = [ctx.enter_context(nc.psum_tensor(f"y_ps{i}", [P, 512], F32)) for i in range(NBANK)]
        stat_ps = ctx.enter_context(nc.psum_tensor("stat_ps", [P, 512], F32))

        conv_in = sem("conv_in")
        const_in = sem("const_in")
        x_in = [[sem(f"x_in_{h}_{k}") for k in range(NCH)] for h in range(2)]
        w_ready = sem("w_ready")
        mv_ready = sem("mv_ready")
        gm_ready = sem("gm_ready")
        ge_ready = sem("ge_ready")
        gv_ready = sem("gv_ready")
        var_ready = sem("var_ready")
        std_ready = sem("std_ready")
        coef_ready = sem("coef_ready")
        g_ready = sem("g_ready")
        hi_ready = sem("hi_ready")
        lo_ready = sem("lo_ready")
        y_done = sem("y_done")
        y_moved = sem("y_moved")
        y_counted = sem("y_counted")
        y_out = [sem(f"y_out_{i}") for i in range(2)]
        dve_link = sem("dve_link")
        bvar_ready = sem("bvar_ready")
        bstd_ready = sem("bstd_ready")
        bn_ready = sem("bn_ready")
        xy_in = [sem(f"xy_in_{i}") for i in range(CT)]
        relu_ready = sem("relu_ready")
        sum_ready = sem("sum_ready")
        out_done = [sem(f"out_done_{i}") for i in range(CT)]

        block = ctx.enter_context(nc.Block())

        def cols(k):
            return slice(k * N, (k + 1) * N)

        @block.sync
        def _(sp):
            sp.dma_start(taps[:, :], conv_rows).then_inc(conv_in, 16)
            sp.dma_start(hankel[:, :], hankel_src).then_inc(conv_in, 16)
            sp.dma_start(gavg[:, :], group_avg).then_inc(const_in, 16)
            with nc.allow_non_contiguous_dma(reason="two vectors of 512 values"):
                sp.dma_start(gam[:, :], gamma.rearrange("(t p) -> p t", p=P)).then_inc(const_in, 16)
                sp.dma_start(bet[:, :], beta.rearrange("(t p) -> p t", p=P)).then_inc(const_in, 16)

            def load_x(image, h, k):
                sp.dma_start(xbuf[:, h, :, cols(k)], x_v[image][:, :, cols(k)]).then_inc(x_in[h][k], 16)

            def store_y(image, k, parity, n):
                sp.wait_ge(y_moved, CT * (n + 1))
                sp.dma_start(y_v[image][:, :, cols(k)], y_sb[:, parity]).then_inc(y_out[parity], 16)

            for l in range(U):
                load_x(l // NCH, l // NCH, l % NCH)

            def pair(j, first=False, last=False):
                for l in range(U):
                    h, k = l // NCH, l % NCH
                    n = U * j + l
                    if not (first and l < 2):
                        c = (l - 2) % U
                        store_y(2 * j + (l - 2) // NCH, c % NCH, l % 2, n - 2)
                    if not last:
                        sp.wait_ge(lo_ready, n + 1)
                        load_x(2 * j + 2 + h, h, k)

            pair(0, first=True)
            with sp.Fori(1, PAIRS - 1) as j:
                pair(j)
            pair(PAIRS - 1, last=True)
            for l in range(U - 2, U):
                store_y(B - 1, l % NCH, l % 2, U * (PAIRS - 1) + l)

            for parity in range(2):
                sp.wait_ge(y_out[parity], 16 * (NCH * PAIRS))

            def load_xy(image, ct, first=False):
                if not first:
                    sp.wait_ge(sum_ready, CT * (image - 1) + ct + 1)
                sp.dma_start(xbuf[:, 0, ct], x_v[image][:, ct]).then_inc(xy_in[ct], 16)
                if not first:
                    sp.wait_ge(out_done[ct], 16 * image)
                sp.dma_start(xbuf[:, 1, ct], y_v[image][:, ct]).then_inc(xy_in[ct], 16)

            sp.wait_ge(lo_ready, U * PAIRS)
            for ct in range(CT):
                load_xy(0, ct, first=True)
            with sp.Fori(1, B) as i:
                for ct in range(CT):
                    load_xy(i, ct)
            for ct in range(CT):
                sp.wait_ge(out_done[ct], 16 * B)

        @block.vector
        def _(dve):
            v = nc.vector
            links = [0, 0]

            def link(ins):
                links[1] += 1
                ins.then_inc(dve_link, 1)
                dve.wait_ge(dve_link, links[0] + links[1])

            def count_x(h, k, use):
                dve.wait_ge(x_in[h][k], 16 * use)
                for ct in range(CT):
                    last = v.bn_stats(x_stats[:, ct, k, :], xbuf[:, h, ct, cols(k)])
                return last

            def pass_wait(source):
                v.tensor_copy(fence[:, :], source)

            def channel_moments():
                pass_wait(x_stats[:, 0, NCH - 1, 0:1])
                for ct in range(CT):
                    last = v.bn_aggr(x_mv[:, ct, :], x_stats[:, ct, :, :].rearrange("p k s -> p (k s)"))
                last.then_inc(mv_ready, 1)

            def second_moments(image):
                dve.wait_ge(gm_ready, image + 1)
                link(v.tensor_copy(g_mean[:, :], stat_ps[:, 0:CT]))
                link(v.tensor_tensor(dev[:, :], x_mv[:, :, 0], g_mean[:, :], ALU.subtract))
                link(v.tensor_tensor(dev2[:, :], dev[:, :], dev[:, :], ALU.mult))
                v.tensor_tensor(g_e[:, :], x_mv[:, :, 1], dev2[:, :], ALU.add).then_inc(ge_ready, 1)

            def variance(image):
                dve.wait_ge(gv_ready, image + 1)
                v.tensor_scalar(g_var[:, :], stat_ps[:, CT:2 * CT], GN_EPS, None, ALU.add).then_inc(var_ready, 1)

            def newton(r, t, var, std):
                link(v.reciprocal(r, std))
                link(v.tensor_tensor(t, r, r, ALU.mult))
                link(v.tensor_tensor(t, t, var, ALU.mult))
                link(v.tensor_scalar(t, t, -0.5, 1.5, ALU.mult, ALU.add))

            def coefficients(image, h):
                dve.wait_ge(std_ready, image + 1)
                newton(g_r[:, :], g_t[:, :], g_var[:, :], g_std[:, :])
                link(v.scalar_tensor_tensor(coef[:, h, 0, :], g_r[:, :], G_SCALE, g_t[:, :], ALU.mult, ALU.mult))
                v.scalar_tensor_tensor(coef[:, h, 1, :], g_mean[:, :], -1.0, coef[:, h, 0, :],
                                       ALU.mult, ALU.mult).then_inc(coef_ready, 1)

            def make_lo(h, k, parity, n):
                dve.wait_ge(hi_ready, n + 1)
                v.tensor_tensor(split[:, parity, 1], xbuf[:, h, :, cols(k)], split[:, parity, 0],
                                ALU.subtract).then_inc(lo_ready, 1)

            def count_y(k, parity, n):
                dve.wait_ge(y_moved, CT * (n + 1))
                for ot in range(CT):
                    last = v.bn_stats(y_stats[:, ot, k, :], y_sb[:, parity, ot, :])
                last.then_inc(y_counted, 1)

            def image_moments(image, n):
                dve.wait_ge(y_counted, n + 1)
                pass_wait(y_stats[:, 0, NCH - 1, 0:1])
                for ot in range(CT):
                    last = v.bn_aggr(y_mv1[:, ot, :], y_stats[:, ot, :, :].rearrange("p k s -> p (k s)"))
                link(last)
                return v.tensor_copy(y_mv[:, :, image, :], y_mv1[:, :, :])

            dve.wait_ge(conv_in, 32)
            link(v.tensor_reduce(w_scale[:, 0:1], taps[:, :], AX_X, ALU.max, apply_absolute_value=True))
            link(v.tensor_scalar(w_scale[:, 0:1], w_scale[:, 0:1], 1e-15, 1.0 / W_MAX, ALU.max, ALU.mult))
            link(v.reciprocal(w_scale[:, 1:2], w_scale[:, 0:1]))
            link(v.tensor_scalar(hankel[:, :], hankel[:, :], w_scale[:, 1:2], None, ALU.mult))
            link(v.tensor_copy(w_hi[:, :], hankel[:, :]))
            v.tensor_tensor(w_lo[:, :], hankel[:, :], w_hi[:, :], ALU.subtract).then_inc(w_ready, 1)
            link(v.tensor_scalar(w_scale[:, 3:4], w_scale[:, 1:2], G_SCALE, None, ALU.mult))
            link(v.tensor_tensor(w_scale[:, 2:3], w_scale[:, 3:4], w_scale[:, 3:4], ALU.mult))
            link(v.tensor_scalar(w_scale[:, 2:3], w_scale[:, 2:3], BN_EPS, None, ALU.mult))

            for k in range(NCH):
                last = count_x(0, k, 1)
            link(last)
            channel_moments()
            second_moments(0)
            variance(0)
            coefficients(0, 0)
            links[0], links[1] = links[0] + links[1], 0
            prologue_links = links[0] - 1

            PER_IMAGE = 1 + 3 + 4 + 1 + 1

            def pair(j, first=False, last=False):
                for l in range(U):
                    h, k = l // NCH, l % NCH
                    n = U * j + l
                    image = 2 * j + h
                    if k == 0:
                        links[0], links[1] = prologue_links + PER_IMAGE * image, int(first and h == 0)
                    if not (last and h == 1):
                        use = j + 1 + h
                        for kx in range(2 * k, min(2 * k + 2, NCH)):
                            stats = count_x(1 - h, kx, use)
                        if k == 3:
                            link(stats)
                            channel_moments()
                        if k == 4:
                            second_moments(image + 1)
                        if k == 5:
                            variance(image + 1)
                        if k == 6:
                            coefficients(image + 1, 1 - h)
                            assert links[1] == PER_IMAGE
                    make_lo(h, k, l % 2, n)
                    if not (first and l < 2):
                        count_y((l - 2) % NCH, l % 2, n - 2)
                    if k == 1 and not (first and h == 0):
                        image_moments(image - 1, n - 2)

            pair(0, first=True)
            with dve.Fori(1, PAIRS - 1) as j:
                pair(j)
            pair(PAIRS - 1, last=True)
            for l in range(U - 2, U):
                count_y(l % NCH, l % 2, U * (PAIRS - 1) + l)
            links[0], links[1] = prologue_links + PER_IMAGE * (B - 1) + 1, 0
            link(image_moments(B - 1, U * PAIRS - 1))

            for ot in range(CT):
                last = v.bn_stats(m_stats[:, ot, :], y_mv[:, ot, :, 0])
            link(last)
            for ot in range(CT):
                v.bn_aggr(m_mv[:, ot, :], m_stats[:, ot, :])
            link(v.tensor_reduce(v_sum[:, :], y_mv[:, :, :, 1], AX_X, ALU.add))
            link(v.scalar_tensor_tensor(b_var[:, :], v_sum[:, :], 1.0 / B, m_mv[:, :, 1], ALU.mult, ALU.add))
            v.tensor_scalar(b_var[:, :], b_var[:, :], w_scale[:, 2:3], None, ALU.add).then_inc(bvar_ready, 1)
            dve.wait_ge(bstd_ready, 1)
            newton(b_r[:, :], b_t[:, :], b_var[:, :], b_std[:, :])
            dve.wait_ge(const_in, 48)
            link(v.tensor_tensor(b_r[:, :], b_r[:, :], b_t[:, :], ALU.mult))
            link(v.tensor_tensor(bn_a[:, :], b_r[:, :], gam[:, :], ALU.mult))
            link(v.tensor_tensor(b_t[:, :], m_mv[:, :, 0], bn_a[:, :], ALU.mult))
            v.tensor_tensor(bn_b[:, :], bet[:, :], b_t[:, :], ALU.subtract).then_inc(bn_ready, 1)

            with dve.Fori(0, B) as i:
                for ct in range(CT):
                    dve.wait_ge(relu_ready, CT * i + ct + 1)
                    v.tensor_tensor(xbuf[:, 1, ct], xbuf[:, 1, ct], xbuf[:, 0, ct],
                                    ALU.add).then_inc(sum_ready, 1)

        @block.scalar
        def _(act):
            a = nc.scalar

            def std(image):
                act.wait_ge(var_ready, image + 1)
                a.activation(g_std[:, :], g_var[:, :], ACT.Sqrt).then_inc(std_ready, 1)

            def normalise(h, k, n):
                for ct in range(CT):
                    last = a.activation(xbuf[:, h, ct, cols(k)], xbuf[:, h, ct, cols(k)], ACT.Identity,
                                        bias=coef[:, h, 1, ct:ct + 1], scale=coef[:, h, 0, ct:ct + 1])
                last.then_inc(g_ready, 1)

            def make_hi(h, k, parity, n, free):
                act.wait_ge(g_ready, n + 1)
                if free:
                    act.wait_ge(y_done, CT * (n - 1))
                a.copy(split[:, parity, 0], xbuf[:, h, :, cols(k)]).then_inc(hi_ready, 1)

            def move_y(l, n, turn, reused):
                parity = l % 2
                if reused:
                    act.wait_ge(y_out[parity], 16 * turn)
                    act.wait_ge(y_counted, n - 1)
                for ot in range(CT):
                    act.wait_ge(y_done, CT * n + ot + 1)
                    a.copy(y_sb[:, parity, ot, :], banks[(CT * l + ot) % NBANK][:, 0:N]).then_inc(y_moved, 1)

            std(0)

            def pair(j, first=False, last=False):
                for l in range(U):
                    h, k = l // NCH, l % NCH
                    n = U * j + l
                    if k == 0:
                        act.wait_ge(coef_ready, 2 * j + h + 1)
                    normalise(h, k, n)
                    early = first and l < 2
                    if not early:
                        turn = NCH * j + (l - 2) // 2
                        move_y((l - 2) % U, n - 2, turn, not (first and l < 4))
                    make_hi(h, k, l % 2, n, not early)
                    if k == 5 and not (last and h == 1):
                        std(2 * j + h + 1)

            pair(0, first=True)
            with act.Fori(1, PAIRS - 1) as j:
                pair(j)
            pair(PAIRS - 1, last=True)
            for l in range(U - 2, U):
                move_y(l, U * (PAIRS - 1) + l, NCH * (PAIRS - 1) + l // 2, True)

            act.wait_ge(bvar_ready, 1)
            a.activation(b_std[:, :], b_var[:, :], ACT.Sqrt).then_inc(bstd_ready, 1)

            act.wait_ge(bn_ready, 1)

            def relu(image, ct):
                act.wait_ge(xy_in[ct], 32 * (image + 1))
                a.activation(xbuf[:, 1, ct], xbuf[:, 1, ct], ACT.Relu, bias=bn_b[:, ct:ct + 1],
                             scale=bn_a[:, ct:ct + 1]).then_inc(relu_ready, 1)

            def store(image, ct):
                act.wait_ge(sum_ready, CT * image + ct + 1)
                act.dma_start(out_v[image][:, ct], xbuf[:, 1, ct]).then_inc(out_done[ct], 16)

            relu(0, 0)
            for ct in range(1, CT):
                relu(0, ct)
                store(0, ct - 1)
            with act.Fori(1, B) as i:
                for ct in range(CT):
                    if ct == 0:
                        store(i - 1, CT - 1)
                        relu(i, ct)
                    else:
                        relu(i, ct)
                        store(i, ct - 1)
            store(B - 1, CT - 1)

        @block.tensor
        def _(pe):
            t = nc.tensor

            def group_means(image):
                pe.wait_ge(mv_ready, image + 1)
                t.matmul(stat_ps[:, 0:CT], gavg[:, :], x_mv[:, :, 0], start=True, stop=True).then_inc(gm_ready, 1)

            def group_variances(image):
                pe.wait_ge(ge_ready, image + 1)
                t.matmul(stat_ps[:, CT:2 * CT], gavg[:, :], g_e[:, :], start=True, stop=True).then_inc(gv_ready, 1)

            def products(l, n, first):
                parity = l % 2
                pe.wait_ge(lo_ready, n + 1)
                for ot in range(CT):
                    if not (first and CT * l + ot < NBANK):
                        pe.wait_ge(y_moved, CT * n + ot + 1 - NBANK)
                    ps = banks[(CT * l + ot) % NBANK][:, 0:N]
                    for ct in range(CT):
                        tile = slice((ct + ot) * P, (ct + ot + 1) * P)
                        hi, lo = split[:, parity, 0, ct, :], split[:, parity, 1, ct, :]
                        t.matmul(ps, w_hi[:, tile], hi, start=(ct == 0), stop=False)
                        t.matmul(ps, w_hi[:, tile], lo, start=False, stop=False)
                        mm = t.matmul(ps, w_lo[:, tile], hi, start=False, stop=(ct == CT - 1))
                    mm.then_inc(y_done, 1)

            pe.wait_ge(const_in, 48)
            group_means(0)
            group_variances(0)
            pe.wait_ge(w_ready, 1)

            def pair(j, first=False, last=False):
                for l in range(U):
                    h, k = l // NCH, l % NCH
                    if k == 3 and not (last and h == 1):
                        group_means(2 * j + h + 1)
                    if k == 4 and not (last and h == 1):
                        group_variances(2 * j + h + 1)
                    products(l, U * j + l, first)

            pair(0, first=True)
            with pe.Fori(1, PAIRS - 1) as j:
                pair(j)
            pair(PAIRS - 1, last=True)


def kernel(x, L0_conv_conv, L0_conv_gamma, L0_conv_beta):
    import concourse.bacc as bacc
    from concourse.bass_utils import run_bass_kernel_spmd

    B, C, H, W = x.shape
    members = C // GROUPS
    group_avg = np.kron(np.eye(P // members), np.full((members, members), 1.0 / members)).astype(np.float32)
    arrays = {
        "x": np.ascontiguousarray(x).reshape(B, C, H * W),
        "conv": np.ascontiguousarray(L0_conv_conv).reshape(-1),
        "gamma": np.ascontiguousarray(L0_conv_gamma),
        "beta": np.ascontiguousarray(L0_conv_beta),
        "group_avg": group_avg,
    }
    nc = bacc.Bacc("TRN2", target_bir_lowering=False, num_devices=1)
    aps = [nc.dram_tensor(n, a.shape, F32, kind="ExternalInput").ap() for n, a in arrays.items()]
    out = nc.dram_tensor("out", (B, C, H * W), F32, kind="ExternalOutput").ap()
    conv_block_kernel(nc, *aps, out)
    r = run_bass_kernel_spmd(nc, [arrays], core_ids=[0])
    return r.results[0]["out"].reshape(B, C, H, W)
```

```python
from contextlib import ExitStack

import numpy as np
import concourse.bass as bass
from concourse import mybir

F32 = mybir.dt.float32
F16 = mybir.dt.float16
ALU = mybir.AluOpType
ACT = mybir.ActivationFunctionType
AX_X = mybir.AxisListType.X

P = 128
GROUPS = 32
GN_EPS = 1e-5
BN_EPS = 1e-5
G_SCALE = 64.0
W_MAX = 1024.0
SPILLED = (2, 4, 6, 9, 11, 13)
STORE_LAG = 4


def conv_block_kernel(nc, x, conv, gamma, beta, group_avg, out):
    B, C, S = x.shape
    CT = C // P
    NCH = 7
    N = S // NCH
    PAIRS = B // 2
    U = 2 * NCH
    WCOLS = (2 * CT - 1) * P
    NBANK = 7
    TAPS = conv.shape[0]
    NSP = len(SPILLED)
    FORMED = [l for l in range(U) if l not in SPILLED]
    NF = len(FORMED)
    assert NF % 2 == 0 and FORMED[:2] == [0, 1]
    RESULTS = []
    for l in range(U):
        if l in SPILLED:
            RESULTS.append((l, 0))
        else:
            r = FORMED.index(l) - 2
            RESULTS.append((FORMED[r], 0) if r >= 0 else (FORMED[r + NF], -1))
    PLACE = {l: q + (U if offset else 0) for q, (l, offset) in enumerate(RESULTS)}
    RELEASE = [PLACE[FORMED[r - 2]] + 1 - 2 - (U if r < 2 else 0) for r in range(NF)]

    pairs = "(j h) (t p) s -> j h p t s"
    x_v = x.rearrange(pairs, h=2, p=P)
    out_v = out.rearrange(pairs, h=2, p=P)
    y_scratch = nc.dram_tensor("y_scratch", (PAIRS, NSP, P, CT * N), F32, kind="Internal").ap()
    y_v = y_scratch.rearrange("j i p (t s) -> j i p t s", t=CT)
    hankel_src = bass.AP(conv.tensor, 0, [[1, P], [1, WCOLS]])
    conv_rows = bass.AP(conv.tensor, 0, [[0, P], [1, TAPS]])

    with ExitStack() as ctx:
        def sb(name, shape, dt=F32):
            return ctx.enter_context(nc.sbuf_tensor(name, shape, dt))

        def sem(name):
            return ctx.enter_context(nc.semaphore(name))

        xbuf = sb("xbuf", [P, 2, CT, S])
        split = sb("split", [P, 2, 2, CT, N], F16)
        y_sb = sb("y_sb", [P, NSP, CT, N])
        g2 = sb("g2", [P, 2, CT, N])
        r2 = sb("r2", [P, 2, CT, N])
        hankel = sb("hankel", [P, WCOLS])
        taps = sb("taps", [P, TAPS])
        w_hi = sb("w_hi", [P, WCOLS], F16)
        w_lo = sb("w_lo", [P, WCOLS], F16)
        gavg = sb("gavg", [P, P])
        gam = sb("gam", [P, CT])
        bet = sb("bet", [P, CT])
        w_scale = sb("w_scale", [P, 4])
        x_stats = sb("x_stats", [P, CT, NCH, 6])
        x_mv = sb("x_mv", [P, CT, 2])
        g_mean = sb("g_mean", [P, CT])
        dev = sb("dev", [P, CT])
        dev2 = sb("dev2", [P, CT])
        g_e = sb("g_e", [P, CT])
        g_var = sb("g_var", [P, CT])
        g_std = sb("g_std", [P, CT])
        g_r = sb("g_r", [P, CT])
        g_t = sb("g_t", [P, CT])
        coef = sb("coef", [P, 2, 2, CT])
        coef_all = sb("coef_all", [P, B, 2, CT])
        y_stats = sb("y_stats", [P, CT, NCH, 6])
        y_mv = sb("y_mv", [P, CT, B, 2])
        y_mv1 = sb("y_mv1", [P, CT, 2])
        fence = sb("fence", [P, 1])
        m_stats = sb("m_stats", [P, CT, 6])
        m_mv = sb("m_mv", [P, CT, 2])
        v_sum = sb("v_sum", [P, CT])
        b_var = sb("b_var", [P, CT])
        b_std = sb("b_std", [P, CT])
        b_r = sb("b_r", [P, CT])
        b_t = sb("b_t", [P, CT])
        bn_a = sb("bn_a", [P, CT])
        bn_b = sb("bn_b", [P, CT])
        banks = [ctx.enter_context(nc.psum_tensor(f"y_ps{i}", [P, 512], F32)) for i in range(NBANK)]
        stat_ps = ctx.enter_context(nc.psum_tensor("stat_ps", [P, 512], F32))
        banks2 = banks + [stat_ps]

        conv_in = sem("conv_in")
        const_in = sem("const_in")
        x_in = [[sem(f"x_in_{h}_{k}") for k in range(NCH)] for h in range(2)]
        w_ready = sem("w_ready")
        mv_ready = sem("mv_ready")
        gm_ready = sem("gm_ready")
        ge_ready = sem("ge_ready")
        gv_ready = sem("gv_ready")
        var_ready = sem("var_ready")
        std_ready = sem("std_ready")
        coef_ready = sem("coef_ready")
        g_ready = sem("g_ready")
        hi_ready = sem("hi_ready")
        lo_ready = sem("lo_ready")
        y_done = sem("y_done")
        y_moved = sem("y_moved")
        y_counted = sem("y_counted")
        y_out = [sem(f"y_out_{i}") for i in range(NSP)]
        dve_link = sem("dve_link")
        bvar_ready = sem("bvar_ready")
        bstd_ready = sem("bstd_ready")
        bn_ready = sem("bn_ready")
        y_back = [sem(f"y_back_{i}") for i in range(NSP)]
        coef2_ready = sem("coef2_ready")
        g2_ready = sem("g2_ready")
        hi2_ready = sem("hi2_ready")
        lo2_ready = sem("lo2_ready")
        y2_done = sem("y2_done")
        relu_ready = sem("relu_ready")
        spill_link = sem("spill_link")
        sum_ready = sem("sum_ready")
        out_done = [sem(f"out_done_{i}") for i in range(U)]

        block = ctx.enter_context(nc.Block())

        def cols(k):
            return slice(k * N, (k + 1) * N)

        @block.sync
        def _(sp):
            sp.dma_start(taps[:, :], conv_rows).then_inc(conv_in, 16)
            sp.dma_start(hankel[:, :], hankel_src).then_inc(conv_in, 16)
            sp.dma_start(gavg[:, :], group_avg).then_inc(const_in, 16)
            with nc.allow_non_contiguous_dma(reason="two vectors of 512 values"):
                sp.dma_start(gam[:, :], gamma.rearrange("(t p) -> p t", p=P)).then_inc(const_in, 16)
                sp.dma_start(bet[:, :], beta.rearrange("(t p) -> p t", p=P)).then_inc(const_in, 16)

            def at(view, i, base):
                return view[base] if type(i) is int else view[base:][i]

            def chunk(view, i, base, l):
                return at(view, i, base)[l // NCH][:, :, cols(l % NCH)]

            def load_x(i, base, l):
                h, k = l // NCH, l % NCH
                sp.dma_start(xbuf[:, h, :, cols(k)], chunk(x_v, i, base, l)).then_inc(x_in[h][k], 16)

            def store_y(i, base, l):
                slot = SPILLED.index(l)
                sp.wait_ge(y_moved, CT * (NSP * (i + base) + slot + 1))
                sp.dma_start(at(y_v, i, base)[slot], y_sb[:, slot]).then_inc(y_out[slot], 16)

            for l in range(U):
                load_x(0, 0, l)

            def pair(i, base, first=False, last=False):
                for l in range(U):
                    lagged = (l - 2) % U
                    if lagged in SPILLED and not (first and l < 2):
                        store_y(i, base + (l - 2) // U, lagged)
                    sp.wait_ge(lo_ready, U * (i + base) + l + 1)
                    load_x(i, 0 if last else base + 1, l)

            pair(0, 0, first=True)
            with sp.Fori(0, PAIRS - 2) as i:
                pair(i, 1)
            pair(0, PAIRS - 1, last=True)
            for l in range(U - 2, U):
                if l in SPILLED:
                    store_y(0, PAIRS - 1, l)

            def load_y(i, base, slot):
                sp.dma_start(y_sb[:, slot], at(y_v, i, base)[slot]).then_inc(y_back[slot], 16)

            for slot in range(NSP):
                sp.wait_ge(y_out[slot], 16 * PAIRS)
                sp.wait_ge(y_counted, CT * (U * (PAIRS - 1) + SPILLED[slot] + 1))
                load_y(0, 0, slot)

            def store_out(i, base, q):
                l, offset = RESULTS[q]
                sp.wait_ge(sum_ready, U * (i + base) - 2 + q + 1)
                sp.dma_start(chunk(out_v, i, base + offset, l),
                             xbuf[:, l // NCH, :, cols(l % NCH)]).then_inc(out_done[l], 16)

            def reload_x(i, base, l):
                sp.wait_ge(out_done[l], 16 * (i + base))
                load_x(i, base, l)

            def pair2(i, base, first=False, last=False):
                for q in range(U):
                    if first and q < 2:
                        continue
                    store_out(i, base, q)
                    if RESULTS[q][0] in SPILLED and not last:
                        load_y(i, base + 1, SPILLED.index(RESULTS[q][0]))
                    if q >= STORE_LAG and not (first and q < STORE_LAG + 2):
                        l, offset = RESULTS[q - STORE_LAG]
                        if not (last and offset == 0):
                            reload_x(i, base + offset + 1, l)
                    if q < STORE_LAG and not first:
                        l, offset = RESULTS[q - STORE_LAG + U]
                        reload_x(i, base + offset, l)

            pair2(0, 0, first=True)
            with sp.Fori(0, PAIRS - 2) as i:
                pair2(i, 1)
            pair2(0, PAIRS - 1, last=True)
            for q in range(2):
                store_out(0, PAIRS, q)
            for l in range(U):
                sp.wait_ge(out_done[l], 16 * PAIRS)

        @block.vector
        def _(dve):
            v = nc.vector
            links = [0, 0]

            def link(ins):
                links[1] += 1
                ins.then_inc(dve_link, 1)
                dve.wait_ge(dve_link, links[0] + links[1])

            def count_x(h, k, use):
                dve.wait_ge(x_in[h][k], 16 * use)
                for ct in range(CT):
                    last = v.bn_stats(x_stats[:, ct, k, :], xbuf[:, h, ct, cols(k)])
                return last

            def pass_wait(source):
                v.tensor_copy(fence[:, :], source)

            def channel_moments():
                pass_wait(x_stats[:, 0, NCH - 1, 0:1])
                for ct in range(CT):
                    last = v.bn_aggr(x_mv[:, ct, :], x_stats[:, ct, :, :].rearrange("p k s -> p (k s)"))
                last.then_inc(mv_ready, 1)

            def second_moments(image):
                dve.wait_ge(gm_ready, image + 1)
                link(v.tensor_copy(g_mean[:, :], stat_ps[:, 0:CT]))
                link(v.tensor_tensor(dev[:, :], x_mv[:, :, 0], g_mean[:, :], ALU.subtract))
                link(v.tensor_tensor(dev2[:, :], dev[:, :], dev[:, :], ALU.mult))
                v.tensor_tensor(g_e[:, :], x_mv[:, :, 1], dev2[:, :], ALU.add).then_inc(ge_ready, 1)

            def variance(image):
                dve.wait_ge(gv_ready, image + 1)
                v.tensor_scalar(g_var[:, :], stat_ps[:, CT:2 * CT], GN_EPS, None, ALU.add).then_inc(var_ready, 1)

            def newton(r, t, var, std):
                link(v.reciprocal(r, std))
                link(v.tensor_tensor(t, r, r, ALU.mult))
                link(v.tensor_tensor(t, t, var, ALU.mult))
                link(v.tensor_scalar(t, t, -0.5, 1.5, ALU.mult, ALU.add))

            def coefficients(image, h):
                dve.wait_ge(std_ready, image + 1)
                newton(g_r[:, :], g_t[:, :], g_var[:, :], g_std[:, :])
                link(v.scalar_tensor_tensor(coef[:, h, 0, :], g_r[:, :], G_SCALE, g_t[:, :], ALU.mult, ALU.mult))
                link(v.scalar_tensor_tensor(coef[:, h, 1, :], g_mean[:, :], -1.0, coef[:, h, 0, :],
                                            ALU.mult, ALU.mult))
                v.tensor_copy(coef_all[:, image], coef[:, h]).then_inc(coef_ready, 1)

            def make_lo(h, k, parity, n):
                dve.wait_ge(hi_ready, n + 1)
                v.tensor_tensor(split[:, parity, 1], xbuf[:, h, :, cols(k)], split[:, parity, 0],
                                ALU.subtract).then_inc(lo_ready, 1)

            def count_y(j, l):
                for ot in range(CT):
                    block = CT * l + ot
                    if l in SPILLED:
                        slot = SPILLED.index(l)
                        dve.wait_ge(y_moved, CT * (NSP * j + slot) + ot + 1)
                        source = y_sb[:, slot, ot, :]
                    else:
                        dve.wait_ge(y_done, CT * U * j + block + 1)
                        source = banks[block % NBANK][:, 0:N]
                    v.bn_stats(y_stats[:, ot, l % NCH, :], source).then_inc(y_counted, 1)

            def image_moments(image, n):
                dve.wait_ge(y_counted, CT * (n + 1))
                pass_wait(y_stats[:, 0, NCH - 1, 0:1])
                for ot in range(CT):
                    last = v.bn_aggr(y_mv1[:, ot, :], y_stats[:, ot, :, :].rearrange("p k s -> p (k s)"))
                link(last)
                return v.tensor_copy(y_mv[:, :, image, :], y_mv1[:, :, :])

            dve.wait_ge(conv_in, 32)
            link(v.tensor_reduce(w_scale[:, 0:1], taps[:, :], AX_X, ALU.max, apply_absolute_value=True))
            link(v.tensor_scalar(w_scale[:, 0:1], w_scale[:, 0:1], 1e-15, 1.0 / W_MAX, ALU.max, ALU.mult))
            link(v.reciprocal(w_scale[:, 1:2], w_scale[:, 0:1]))
            link(v.tensor_scalar(hankel[:, :], hankel[:, :], w_scale[:, 1:2], None, ALU.mult))
            link(v.tensor_copy(w_hi[:, :], hankel[:, :]))
            v.tensor_tensor(w_lo[:, :], hankel[:, :], w_hi[:, :], ALU.subtract).then_inc(w_ready, 1)
            link(v.tensor_scalar(w_scale[:, 3:4], w_scale[:, 1:2], G_SCALE, None, ALU.mult))
            link(v.tensor_tensor(w_scale[:, 2:3], w_scale[:, 3:4], w_scale[:, 3:4], ALU.mult))
            link(v.tensor_scalar(w_scale[:, 2:3], w_scale[:, 2:3], BN_EPS, None, ALU.mult))

            for k in range(NCH):
                last = count_x(0, k, 1)
            link(last)
            channel_moments()
            second_moments(0)
            variance(0)
            coefficients(0, 0)
            links[0], links[1] = links[0] + links[1], 0
            prologue_links = links[0] - 1

            PER_IMAGE = 1 + 3 + 4 + 2 + 1

            def pair(j, first=False, last=False):
                for l in range(U):
                    h, k = l // NCH, l % NCH
                    n = U * j + l
                    image = 2 * j + h
                    if k == 0:
                        links[0], links[1] = prologue_links + PER_IMAGE * image, int(first and h == 0)
                    if not (last and h == 1):
                        use = j + 1 + h
                        for kx in range(2 * k, min(2 * k + 2, NCH)):
                            stats = count_x(1 - h, kx, use)
                        if k == 3:
                            link(stats)
                            channel_moments()
                        if k == 4:
                            second_moments(image + 1)
                        if k == 5:
                            variance(image + 1)
                        if k == 6:
                            coefficients(image + 1, 1 - h)
                            assert links[1] == PER_IMAGE
                    if not (first and l < 2):
                        count_y(j + (l - 2) // U, (l - 2) % U)
                    make_lo(h, k, l % 2, n)
                    if k == 1 and not (first and h == 0):
                        image_moments(image - 1, n - 2)

            pair(0, first=True)
            with dve.Fori(1, PAIRS - 1) as j:
                pair(j)
            pair(PAIRS - 1, last=True)
            for l in range(U - 2, U):
                count_y(PAIRS - 1, l)
            links[0], links[1] = prologue_links + PER_IMAGE * (B - 1) + 1, 0
            link(image_moments(B - 1, U * PAIRS - 1))

            for ot in range(CT):
                last = v.bn_stats(m_stats[:, ot, :], y_mv[:, ot, :, 0])
            link(last)
            for ot in range(CT):
                v.bn_aggr(m_mv[:, ot, :], m_stats[:, ot, :])
            link(v.tensor_reduce(v_sum[:, :], y_mv[:, :, :, 1], AX_X, ALU.add))
            link(v.scalar_tensor_tensor(b_var[:, :], v_sum[:, :], 1.0 / B, m_mv[:, :, 1], ALU.mult, ALU.add))
            v.tensor_scalar(b_var[:, :], b_var[:, :], w_scale[:, 2:3], None, ALU.add).then_inc(bvar_ready, 1)

            def batch_coefficients():
                dve.wait_ge(bstd_ready, 1)
                newton(b_r[:, :], b_t[:, :], b_var[:, :], b_std[:, :])
                dve.wait_ge(const_in, 48)
                link(v.tensor_tensor(b_r[:, :], b_r[:, :], b_t[:, :], ALU.mult))
                link(v.tensor_tensor(bn_a[:, :], b_r[:, :], gam[:, :], ALU.mult))
                link(v.tensor_tensor(b_t[:, :], m_mv[:, :, 0], bn_a[:, :], ALU.mult))
                link(v.tensor_tensor(bn_b[:, :], bet[:, :], b_t[:, :], ALU.subtract))
                v.tensor_copy(fence[:, :], bn_b[:, 0:1]).then_inc(bn_ready, 1)

            def make_lo2(r, parity):
                dve.wait_ge(hi2_ready, r + 1)
                v.tensor_tensor(split[:, parity, 1], g2[:, parity], split[:, parity, 0],
                                ALU.subtract).then_inc(lo2_ready, 1)

            def add_formed(j, l):
                h, k, r = l // NCH, l % NCH, FORMED.index(l)
                dve.wait_ge(relu_ready, CT * (NF * j + r + 1))
                v.tensor_tensor(xbuf[:, h, :, cols(k)], xbuf[:, h, :, cols(k)], r2[:, r % 2],
                                ALU.add).then_inc(sum_ready, 1)

            def add_spilled(j, l):
                h, k, slot = l // NCH, l % NCH, SPILLED.index(l)
                dve.wait_ge(y_back[slot], 16 * (j + 1))
                for ct in range(CT):
                    last = v.tensor_scalar(y_sb[:, slot, ct, :], y_sb[:, slot, ct, :], bn_a[:, ct:ct + 1],
                                           bn_b[:, ct:ct + 1], ALU.mult, ALU.add)
                last.then_inc(spill_link, 1)
                dve.wait_ge(spill_link, NSP * j + slot + 1)
                dve.wait_ge(x_in[h][k], 16 * (PAIRS + j + 1))
                v.scalar_tensor_tensor(xbuf[:, h, :, cols(k)], y_sb[:, slot], 0.0, xbuf[:, h, :, cols(k)],
                                       ALU.max, ALU.add).then_inc(sum_ready, 1)

            def pair2(j, first=False):
                for l in range(U):
                    done, offset = RESULTS[l]
                    if l in SPILLED:
                        add_spilled(j, l)
                        continue
                    r = FORMED.index(l)
                    if not (first and r < 2):
                        add_formed(j + offset, done)
                    make_lo2(NF * j + r, r % 2)
                    if first and r == 0:
                        batch_coefficients()

            pair2(0, first=True)
            with dve.Fori(1, PAIRS) as j:
                pair2(j)
            for l in FORMED[-2:]:
                add_formed(PAIRS - 1, l)

        @block.scalar
        def _(act):
            a = nc.scalar

            def std(image):
                act.wait_ge(var_ready, image + 1)
                a.activation(g_std[:, :], g_var[:, :], ACT.Sqrt).then_inc(std_ready, 1)

            def normalise(h, k, n):
                for ct in range(CT):
                    last = a.activation(xbuf[:, h, ct, cols(k)], xbuf[:, h, ct, cols(k)], ACT.Identity,
                                        bias=coef[:, h, 1, ct:ct + 1], scale=coef[:, h, 0, ct:ct + 1])
                last.then_inc(g_ready, 1)

            def make_hi(h, k, parity, n, free):
                act.wait_ge(g_ready, n + 1)
                if free:
                    act.wait_ge(y_done, CT * (n - 1))
                a.copy(split[:, parity, 0], xbuf[:, h, :, cols(k)]).then_inc(hi_ready, 1)

            def move_y(j, l, reused):
                slot = SPILLED.index(l)
                if reused:
                    act.wait_ge(y_out[slot], 16 * j)
                    act.wait_ge(y_counted, CT * (U * (j - 1) + l + 1))
                for ot in range(CT):
                    block = CT * l + ot
                    act.wait_ge(y_done, CT * U * j + block + 1)
                    a.copy(y_sb[:, slot, ot, :], banks[block % NBANK][:, 0:N]).then_inc(y_moved, 1)

            std(0)

            def pair(j, first=False, last=False):
                for l in range(U):
                    h, k = l // NCH, l % NCH
                    n = U * j + l
                    if k == 0:
                        act.wait_ge(coef_ready, 2 * j + h + 1)
                    normalise(h, k, n)
                    early = first and l < 2
                    if (l - 2) % U in SPILLED and not early:
                        move_y(j + (l - 2) // U, (l - 2) % U, not (first and l >= 2))
                    make_hi(h, k, l % 2, n, not early)
                    if k == 5 and not (last and h == 1):
                        std(2 * j + h + 1)

            pair(0, first=True)
            with act.Fori(1, PAIRS - 1) as j:
                pair(j)
            pair(PAIRS - 1, last=True)
            for l in range(U - 2, U):
                if l in SPILLED:
                    move_y(PAIRS - 1, l, True)

            def fetch_coefficients(image, h):
                a.copy(coef[:, h], coef_all[:, image]).then_inc(coef2_ready, 1)

            def normalise2(j, l):
                h, k, r = l // NCH, l % NCH, FORMED.index(l)
                act.wait_ge(x_in[h][k], 16 * (PAIRS + j + 1))
                for ct in range(CT):
                    last = a.activation(g2[:, r % 2, ct, :], xbuf[:, h, ct, cols(k)], ACT.Identity,
                                        bias=coef[:, h, 1, ct:ct + 1], scale=coef[:, h, 0, ct:ct + 1])
                last.then_inc(g2_ready, 1)

            def make_hi2(n, parity, early):
                act.wait_ge(g2_ready, n + 1)
                if not early:
                    act.wait_ge(y2_done, CT * (n - 1))
                a.copy(split[:, parity, 0], g2[:, parity]).then_inc(hi2_ready, 1)

            def relu(j, l, early):
                r = FORMED.index(l)
                n = NF * j + r
                if not early:
                    act.wait_ge(sum_ready, U * j + RELEASE[r])
                for ot in range(CT):
                    block = CT * r + ot
                    act.wait_ge(y2_done, CT * n + ot + 1)
                    a.activation(r2[:, r % 2, ot, :], banks2[block % len(banks2)][:, 0:N], ACT.Relu,
                                 bias=bn_b[:, ot:ot + 1], scale=bn_a[:, ot:ot + 1]).then_inc(relu_ready, 1)

            def pair2(j, first=False):
                for l in FORMED:
                    h, r = l // NCH, FORMED.index(l)
                    if r == 0 or FORMED[r - 1] // NCH != h:
                        fetch_coefficients(2 * j + h, h)
                        act.wait_ge(coef2_ready, 2 * j + h + 1)
                    n = NF * j + r
                    if not (first and r < 2):
                        act.wait_ge(lo2_ready, n - 1)
                    normalise2(j, l)
                    if first and r == 2:
                        act.wait_ge(bn_ready, 1)
                    if not (first and r < 2):
                        done, offset = RESULTS[l]
                        relu(j + offset, done, first and r < 4)
                    make_hi2(n, r % 2, first and r < 2)
                    if first and r == 0:
                        act.wait_ge(bvar_ready, 1)
                        a.activation(b_std[:, :], b_var[:, :], ACT.Sqrt).then_inc(bstd_ready, 1)

            act.wait_ge(y_done, CT * U * PAIRS)
            pair2(0, first=True)
            with act.Fori(1, PAIRS) as j:
                pair2(j)
            for l in FORMED[-2:]:
                relu(PAIRS - 1, l, False)

        @block.tensor
        def _(pe):
            t = nc.tensor

            def group_means(image):
                pe.wait_ge(mv_ready, image + 1)
                t.matmul(stat_ps[:, 0:CT], gavg[:, :], x_mv[:, :, 0], start=True, stop=True).then_inc(gm_ready, 1)

            def group_variances(image):
                pe.wait_ge(ge_ready, image + 1)
                t.matmul(stat_ps[:, CT:2 * CT], gavg[:, :], g_e[:, :], start=True, stop=True).then_inc(gv_ready, 1)

            def form(ps, parity, ot):
                for ct in range(CT):
                    tile = slice((ct + ot) * P, (ct + ot + 1) * P)
                    hi, lo = split[:, parity, 0, ct, :], split[:, parity, 1, ct, :]
                    t.matmul(ps, w_hi[:, tile], hi, start=(ct == 0), stop=False)
                    t.matmul(ps, w_hi[:, tile], lo, start=False, stop=False)
                    last = t.matmul(ps, w_lo[:, tile], hi, start=False, stop=(ct == CT - 1))
                return last

            def products(j, l, first):
                parity, n = l % 2, U * j + l
                pe.wait_ge(lo_ready, n + 1)
                for ot in range(CT):
                    block = CT * l + ot
                    if not (first and block < NBANK):
                        old, turn = (block - NBANK) % (CT * U), j + (block - NBANK) // (CT * U)
                        if old // CT in SPILLED:
                            pe.wait_ge(y_moved, CT * (NSP * turn + SPILLED.index(old // CT)) + old % CT + 1)
                        else:
                            pe.wait_ge(y_counted, CT * U * turn + old + 1)
                    form(banks[block % NBANK][:, 0:N], parity, ot).then_inc(y_done, 1)

            def products2(r, n, early):
                pe.wait_ge(lo2_ready, n + 1)
                for ot in range(CT):
                    block = CT * r + ot
                    if not (early and block < len(banks2)):
                        pe.wait_ge(relu_ready, CT * n + ot + 1 - len(banks2))
                    form(banks2[block % len(banks2)][:, 0:N], r % 2, ot).then_inc(y2_done, 1)

            pe.wait_ge(const_in, 48)
            group_means(0)
            group_variances(0)
            pe.wait_ge(w_ready, 1)

            def pair(j, first=False, last=False):
                for l in range(U):
                    h, k = l // NCH, l % NCH
                    if k == 3 and not (last and h == 1):
                        group_means(2 * j + h + 1)
                    if k == 4 and not (last and h == 1):
                        group_variances(2 * j + h + 1)
                    products(j, l, first)

            pair(0, first=True)
            with pe.Fori(1, PAIRS - 1) as j:
                pair(j)
            pair(PAIRS - 1, last=True)

            pe.wait_ge(y_counted, CT * U * PAIRS)
            pe.wait_ge(y_moved, CT * NSP * PAIRS)

            def pair2(j, first=False):
                for r in range(NF):
                    products2(r, NF * j + r, first)

            pair2(0, first=True)
            with pe.Fori(1, PAIRS) as j:
                pair2(j)


def kernel(x, L0_conv_conv, L0_conv_gamma, L0_conv_beta):
    import concourse.bacc as bacc
    from concourse.bass_utils import run_bass_kernel_spmd

    B, C, H, W = x.shape
    members = C // GROUPS
    group_avg = np.kron(np.eye(P // members), np.full((members, members), 1.0 / members)).astype(np.float32)
    arrays = {
        "x": np.ascontiguousarray(x).reshape(B, C, H * W),
        "conv": np.ascontiguousarray(L0_conv_conv).reshape(-1),
        "gamma": np.ascontiguousarray(L0_conv_gamma),
        "beta": np.ascontiguousarray(L0_conv_beta),
        "group_avg": group_avg,
    }
    nc = bacc.Bacc("TRN2", target_bir_lowering=False, num_devices=1)
    aps = [nc.dram_tensor(n, a.shape, F32, kind="ExternalInput").ap() for n, a in arrays.items()]
    out = nc.dram_tensor("out", (B, C, H * W), F32, kind="ExternalOutput").ap()
    conv_block_kernel(nc, *aps, out)
    r = run_bass_kernel_spmd(nc, [arrays], core_ids=[0])
    return r.results[0]["out"].reshape(B, C, H, W)
```

```python
from contextlib import ExitStack

import numpy as np
import concourse.bass as bass
from concourse import mybir

F32 = mybir.dt.float32
F16 = mybir.dt.float16
ALU = mybir.AluOpType
ACT = mybir.ActivationFunctionType
AX_X = mybir.AxisListType.X

P = 128
GROUPS = 32
GN_EPS = 1e-5
BN_EPS = 1e-5
G_SCALE = 64.0
W_MAX = 1024.0
SPILLED = (4, 11)
LO_DVE = 2
LO_DVE2 = 3
AHEAD = 12
STORE_LAG = 4


def conv_block_kernel(nc, x, conv, gamma, beta, group_avg, out):
    B, C, S = x.shape
    CT = C // P
    NCH = 7
    N = S // NCH
    PAIRS = B // 2
    U = 2 * NCH
    WCOLS = (2 * CT - 1) * P
    DCOLS = (CT - 1) * P
    NBANK, NBANK2 = 7, 8
    TAPS = conv.shape[0]
    NSP = len(SPILLED)
    FORMED = [l for l in range(U) if l not in SPILLED]
    NF = len(FORMED)
    CH = CT // 2
    YS = 2
    YT = NSP // YS
    SPLITS = 4
    short, rounds = -U % SPLITS, -(-U // SPLITS)
    PLACES = [p for i in range(rounds) for p in range(SPLITS - (i >= rounds - short))]
    LAST = (NCH - 1 - AHEAD) % NCH
    assert NSP % YS == 0 and CT * U % NBANK == 0 and CT * NF % NBANK2 == 0
    assert NF % 2 == 0 and NF % SPLITS == 0 and len(PLACES) == U and FORMED[:2] == [0, 1]
    RESULTS = []
    for l in range(U):
        if l in SPILLED:
            RESULTS.append((l, 0))
        else:
            r = FORMED.index(l) - 2
            RESULTS.append((FORMED[r], 0) if r >= 0 else (FORMED[r + NF], -1))
    PLACE = {l: q + (U if offset else 0) for q, (l, offset) in enumerate(RESULTS)}
    RELEASE = [PLACE[FORMED[r - 2]] + 1 - 2 - (U if r < 2 else 0) for r in range(NF)]

    pairs = "(j h) (t p) s -> j h p t s"
    x_v = x.rearrange(pairs, h=2, p=P)
    out_v = out.rearrange(pairs, h=2, p=P)
    y_scratch = nc.dram_tensor("y_scratch", (PAIRS, NSP, P, CT * N), F32, kind="Internal").ap()
    y_v = y_scratch.rearrange("j i p (t s) -> j i p t s", t=CT)
    hankel_src = bass.AP(conv.tensor, 0, [[1, P], [1, WCOLS]])
    conv_rows = bass.AP(conv.tensor, 0, [[0, P], [1, TAPS]])

    with ExitStack() as ctx:
        def sb(name, shape, dt=F32):
            return ctx.enter_context(nc.sbuf_tensor(name, shape, dt))

        def sem(name):
            return ctx.enter_context(nc.semaphore(name))

        xbuf = sb("xbuf", [P, 2, CT, S])
        split = sb("split", [P, SPLITS, 2, CT + CH, N], F16)
        y_sb = sb("y_sb", [P, YS, CT, N])
        work = sb("work", [P, 5 * CT * N])
        hankel = work[:, 0:WCOLS]
        diffs = work[:, WCOLS:WCOLS + 2 * DCOLS].rearrange("p (a u) -> p a u", a=2)
        taps = work[:, WCOLS + 2 * DCOLS:WCOLS + 2 * DCOLS + TAPS]
        chunks = work[:, :].rearrange("p (i t n) -> p i t n", i=5, t=CT)
        assert WCOLS + 2 * DCOLS + TAPS <= 4 * CT * N
        x_sum = chunks[:, 4].rearrange("p (a t) n -> p a t n", a=2)
        g2 = chunks[:, 0:2]
        r2 = chunks[:, 2:4]
        x_sum2 = chunks[:, 4].rearrange("p (a t) n -> p a t n", a=2)
        w_hi = sb("w_hi", [P, WCOLS], F16)
        w_lo = sb("w_lo", [P, WCOLS], F16)
        d_hi = sb("d_hi", [P, 2, DCOLS], F16)
        d_lo = sb("d_lo", [P, 2, DCOLS], F16)
        gavg = sb("gavg", [P, P])
        gam = sb("gam", [P, CT])
        bet = sb("bet", [P, CT])
        w_scale = sb("w_scale", [P, 4])
        x_stats = sb("x_stats", [P, 2, CT, NCH, 6])
        x_mv = sb("x_mv", [P, CT, 2])
        g_mean = sb("g_mean", [P, CT])
        dev = sb("dev", [P, CT])
        dev2 = sb("dev2", [P, CT])
        g_e = sb("g_e", [P, CT])
        g_var = sb("g_var", [P, CT])
        g_std = sb("g_std", [P, CT])
        g_r = sb("g_r", [P, CT])
        g_t = sb("g_t", [P, CT])
        coef = sb("coef", [P, 2, 2, CT])
        coef_all = sb("coef_all", [P, B, 2, CT])
        y_stats = sb("y_stats", [P, CT, NCH, 6])
        y_mv = sb("y_mv", [P, CT, B, 2])
        y_mv1 = sb("y_mv1", [P, CT, 2])
        fence = sb("fence", [P, 1])
        m_stats = sb("m_stats", [P, CT, 6])
        m_mv = sb("m_mv", [P, CT, 2])
        v_sum = sb("v_sum", [P, CT])
        b_var = sb("b_var", [P, CT])
        b_std = sb("b_std", [P, CT])
        b_r = sb("b_r", [P, CT])
        b_t = sb("b_t", [P, CT])
        bn_a = sb("bn_a", [P, CT])
        bn_b = sb("bn_b", [P, CT])
        banks = [ctx.enter_context(nc.psum_tensor(f"y_ps{i}", [P, 512], F32)) for i in range(NBANK)]
        stat_ps = ctx.enter_context(nc.psum_tensor("stat_ps", [P, 512], F32))
        banks2 = [stat_ps] + banks

        conv_in = sem("conv_in")
        const_in = sem("const_in")
        x_in = [[sem(f"x_in_{h}_{k}") for k in range(NCH)] for h in range(2)]
        w_ready = sem("w_ready")
        mv_ready = sem("mv_ready")
        gm_ready = sem("gm_ready")
        ge_ready = sem("ge_ready")
        gv_ready = sem("gv_ready")
        var_ready = sem("var_ready")
        std_ready = sem("std_ready")
        coef_ready = sem("coef_ready")
        g_ready = sem("g_ready")
        hi_ready = sem("hi_ready")
        lo_ready = sem("lo_ready")
        lo1_ready = sem("lo1_ready")
        x_sum_ready = sem("x_sum_ready")
        sum_hi_ready = sem("sum_hi_ready")
        sum_lo_ready = sem("sum_lo_ready")
        both_done = sem("both_done")
        seeded = sem("seeded")
        y_done = sem("y_done")
        y_moved = sem("y_moved")
        y_counted = sem("y_counted")
        y_out = [sem(f"y_out_{i}") for i in range(YS)]
        dve_link = sem("dve_link")
        bvar_ready = sem("bvar_ready")
        bstd_ready = sem("bstd_ready")
        bn_ready = sem("bn_ready")
        y_back = [sem(f"y_back_{i}") for i in range(YS)]
        coef2_ready = sem("coef2_ready")
        g2_ready = sem("g2_ready")
        hi2_ready = sem("hi2_ready")
        lo2_ready = sem("lo2_ready")
        lo3_ready = sem("lo3_ready")
        both2_done = sem("both2_done")
        seeded2 = sem("seeded2")
        y2_done = sem("y2_done")
        x_sum2_ready = sem("x_sum2_ready")
        sum_hi2_ready = sem("sum_hi2_ready")
        sum_lo2_ready = sem("sum_lo2_ready")
        bn_low_ready = sem("bn_low_ready")
        bn_high_ready = sem("bn_high_ready")
        bn_spill_ready = sem("bn_spill_ready")
        sum_ready = sem("sum_ready")
        out_done = [sem(f"out_done_{i}") for i in range(U)]

        block = ctx.enter_context(nc.Block())

        ORDER = [0, 2, 1, 3]

        def bank(l, place):
            return banks[(CT * l + place) % NBANK]

        def bank2(r, place):
            return banks2[(CT * r + place) % NBANK2]

        def wait_r2_free(engine, j, r):
            engine.wait_ge(sum_ready, U * j + RELEASE[r])

        def cols(k):
            return slice(k * N, (k + 1) * N)

        @block.sync
        def _(sp):
            def at(view, i, base):
                return view[base] if type(i) is int else view[base:][i]

            def chunk(view, i, base, l):
                return at(view, i, base)[l // NCH][:, :, cols(l % NCH)]

            def load_x(i, base, l):
                h, k = l // NCH, l % NCH
                sp.dma_start(xbuf[:, h, :, cols(k)], chunk(x_v, i, base, l)).then_inc(x_in[h][k], 16)

            def store_y(i, base, l):
                spill = SPILLED.index(l)
                slot = spill % YS
                sp.wait_ge(y_moved, CT * (NSP * (i + base) + spill + 1))
                sp.dma_start(at(y_v, i, base)[spill], y_sb[:, slot]).then_inc(y_out[slot], 16)

            for l in range(2):
                load_x(0, 0, l)
            sp.dma_start(taps, conv_rows).then_inc(conv_in, 16)
            sp.dma_start(hankel, hankel_src).then_inc(conv_in, 16)
            sp.dma_start(gavg[:, :], group_avg).then_inc(const_in, 16)
            with nc.allow_non_contiguous_dma(reason="two vectors of 512 values"):
                sp.dma_start(gam[:, :], gamma.rearrange("(t p) -> p t", p=P)).then_inc(const_in, 16)
                sp.dma_start(bet[:, :], beta.rearrange("(t p) -> p t", p=P)).then_inc(const_in, 16)
            for l in range(2, U):
                load_x(0, 0, l)

            def pair(i, base, first=False, last=False):
                for l in range(U):
                    lagged = (l - 2) % U
                    if lagged in SPILLED and not (first and l < 2):
                        store_y(i, base + (l - 2) // U, lagged)
                    sp.wait_ge(lo_ready, U * (i + base) + l + 1)
                    sp.wait_ge(lo1_ready, U * (i + base) + l + 1)
                    load_x(i, 0 if last else base + 1, l)

            pair(0, 0, first=True)
            with sp.Fori(0, PAIRS - 2) as i:
                pair(i, 1)
            pair(0, PAIRS - 1, last=True)
            for l in range(U - 2, U):
                if l in SPILLED:
                    store_y(0, PAIRS - 1, l)

            def load_y(i, base, spill):
                sp.dma_start(y_sb[:, spill % YS], at(y_v, i, base)[spill]).then_inc(y_back[spill % YS], 16)

            for slot in range(YS):
                sp.wait_ge(y_out[slot], 16 * YT * PAIRS)
                load_y(0, 0, slot)

            def store_out(i, base, q):
                l, offset = RESULTS[q]
                sp.wait_ge(sum_ready, U * (i + base) - 2 + q + 1)
                sp.dma_start(chunk(out_v, i, base + offset, l),
                             xbuf[:, l // NCH, :, cols(l % NCH)]).then_inc(out_done[l], 16)

            def reload_x(i, base, l):
                sp.wait_ge(out_done[l], 16 * (i + base))
                load_x(i, base, l)

            def pair2(i, base, first=False, last=False):
                for q in range(U):
                    if first and q < 2:
                        continue
                    store_out(i, base, q)
                    if RESULTS[q][0] in SPILLED:
                        spill = SPILLED.index(RESULTS[q][0]) + YS
                        if spill < NSP:
                            load_y(i, base, spill)
                        elif not last:
                            load_y(i, base + 1, spill - NSP)
                    if q >= STORE_LAG and not (first and q < STORE_LAG + 2):
                        l, offset = RESULTS[q - STORE_LAG]
                        if not (last and offset == 0):
                            reload_x(i, base + offset + 1, l)
                    if q < STORE_LAG and not first:
                        l, offset = RESULTS[q - STORE_LAG + U]
                        reload_x(i, base + offset, l)

            pair2(0, 0, first=True)
            with sp.Fori(0, PAIRS - 2) as i:
                pair2(i, 1)
            pair2(0, PAIRS - 1, last=True)
            for q in range(2):
                store_out(0, PAIRS, q)
            for l in range(U):
                sp.wait_ge(out_done[l], 16 * PAIRS)

        @block.vector
        def _(dve):
            v = nc.vector
            links = [0, 0]

            def link(ins):
                links[1] += 1
                ins.then_inc(dve_link, 1)
                dve.wait_ge(dve_link, links[0] + links[1])

            def count_x(j, l):
                h, k = l // NCH, l % NCH
                dve.wait_ge(x_in[h][k], 16 * (j + 1))
                for ct in range(CT):
                    last = v.bn_stats(x_stats[:, h, ct, k, :], xbuf[:, h, ct, cols(k)])
                return last

            def pass_wait(source):
                v.tensor_copy(fence[:, :], source)

            def channel_moments(h):
                pass_wait(x_stats[:, h, 0, NCH - 1, 0:1])
                for ct in range(CT):
                    last = v.bn_aggr(x_mv[:, ct, :], x_stats[:, h, ct, :, :].rearrange("p k s -> p (k s)"))
                last.then_inc(mv_ready, 1)

            def second_moments(image):
                dve.wait_ge(gm_ready, image + 1)
                link(v.tensor_copy(g_mean[:, :], stat_ps[:, 0:CT]))
                link(v.tensor_tensor(dev[:, :], x_mv[:, :, 0], g_mean[:, :], ALU.subtract))
                link(v.tensor_tensor(dev2[:, :], dev[:, :], dev[:, :], ALU.mult))
                v.tensor_tensor(g_e[:, :], x_mv[:, :, 1], dev2[:, :], ALU.add).then_inc(ge_ready, 1)

            def variance(image):
                dve.wait_ge(gv_ready, image + 1)
                v.tensor_scalar(g_var[:, :], stat_ps[:, CT:2 * CT], GN_EPS, None, ALU.add).then_inc(var_ready, 1)

            def newton(r, t, var, std):
                link(v.reciprocal(r, std))
                link(v.tensor_tensor(t, r, r, ALU.mult))
                link(v.tensor_tensor(t, t, var, ALU.mult))
                link(v.tensor_scalar(t, t, -0.5, 1.5, ALU.mult, ALU.add))

            def coefficients(image, h):
                dve.wait_ge(std_ready, image + 1)
                newton(g_r[:, :], g_t[:, :], g_var[:, :], g_std[:, :])
                link(v.scalar_tensor_tensor(coef[:, h, 0, :], g_r[:, :], G_SCALE, g_t[:, :], ALU.mult, ALU.mult))
                link(v.scalar_tensor_tensor(coef[:, h, 1, :], g_mean[:, :], -1.0, coef[:, h, 0, :],
                                            ALU.mult, ALU.mult))
                v.tensor_copy(coef_all[:, image], coef[:, h]).then_inc(coef_ready, 1)

            def make_lo(h, k, place, n):
                dve.wait_ge(hi_ready, n + 1)
                v.tensor_tensor(split[:, place, 1, 0:LO_DVE], xbuf[:, h, 0:LO_DVE, cols(k)],
                                split[:, place, 0, 0:LO_DVE],
                                ALU.subtract).then_inc(lo_ready, 1)

            def count_y(j, l, rows, first=False):
                if l in SPILLED and rows[0] == 0 and not (first and SPILLED.index(l) < YS):
                    spill = SPILLED.index(l)
                    dve.wait_ge(y_out[spill % YS], 16 * (YT * j + spill // YS))
                for place in range(2 * rows[0], 2 * rows[-1] + 2):
                    ot, tile = ORDER[place], CT * (U * j + l) + place
                    ps = bank(l, place)[:, 0:N]
                    dve.wait_ge(y_done, tile + 1)
                    if l in SPILLED:
                        v.tensor_copy(y_sb[:, SPILLED.index(l) % YS, ot, :], ps).then_inc(y_moved, 1)
                    v.bn_stats(y_stats[:, ot, l % NCH, :], ps).then_inc(y_counted, 1)

            def image_moments(image, n):
                dve.wait_ge(y_counted, CT * (n + 1))
                pass_wait(y_stats[:, 0, NCH - 1, 0:1])
                for ot in range(CT):
                    last = v.bn_aggr(y_mv1[:, ot, :], y_stats[:, ot, :, :].rearrange("p k s -> p (k s)"))
                link(last)
                return v.tensor_copy(y_mv[:, :, image, :], y_mv1[:, :, :])

            def scale_kernel():
                dve.wait_ge(conv_in, 32)
                link(v.tensor_reduce(w_scale[:, 0:1], taps, AX_X, ALU.max, apply_absolute_value=True))
                link(v.tensor_scalar(w_scale[:, 0:1], w_scale[:, 0:1], 1e-15, 1.0 / W_MAX, ALU.max, ALU.mult))
                link(v.reciprocal(w_scale[:, 1:2], w_scale[:, 0:1]))
                link(v.tensor_scalar(hankel, hankel, w_scale[:, 1:2], None, ALU.mult))

            def split_kernel():
                v.tensor_tensor(diffs[:, 0], hankel[:, 0:DCOLS], hankel[:, CH * P:CH * P + DCOLS], ALU.subtract)
                v.tensor_tensor(diffs[:, 1], hankel[:, CT * P:CT * P + DCOLS], hankel[:, CH * P:CH * P + DCOLS],
                                ALU.subtract)
                link(v.tensor_copy(w_hi[:, :], hankel))
                link(v.tensor_copy(d_hi[:, :, :], diffs))
                v.tensor_tensor(w_lo[:, :], hankel, w_hi[:, :], ALU.subtract)
                v.tensor_tensor(d_lo[:, :, :], diffs, d_hi[:, :, :], ALU.subtract).then_inc(w_ready, 1)
                link(v.tensor_scalar(w_scale[:, 3:4], w_scale[:, 1:2], G_SCALE, None, ALU.mult))
                link(v.tensor_tensor(w_scale[:, 2:3], w_scale[:, 3:4], w_scale[:, 3:4], ALU.mult))
                link(v.tensor_scalar(w_scale[:, 2:3], w_scale[:, 2:3], BN_EPS, None, ALU.mult))

            for l in range(2):
                count_x(0, l)
            scale_kernel()
            for l in range(2, NCH):
                last = count_x(0, l)
            link(last)
            channel_moments(0)
            second_moments(0)
            variance(0)
            coefficients(0, 0)
            split_kernel()
            EARLY = NCH + 3
            for l in range(NCH, EARLY):
                count_x(0, l)
            links[0], links[1] = links[0] + links[1], 0
            prologue_links = links[0] - 1

            PER_IMAGE = 1 + 3 + 4 + 2 + 1

            def pair(j, first=False, last=False):
                for l in range(U):
                    h, k = l // NCH, l % NCH
                    n = U * j + l
                    image = 2 * j + h
                    if k == 0:
                        links[0], links[1] = prologue_links + PER_IMAGE * image, int(first and h == 0)
                    counted = range(l + AHEAD, l + AHEAD + 1)
                    if first and l <= LAST:
                        left = U - EARLY
                        counted = range(EARLY + left * l // (LAST + 1), EARLY + left * (l + 1) // (LAST + 1))
                    if first and l <= LAST:
                        make_lo(h, k, PLACES[l], n)
                    for c in counted:
                        if not (last and c >= U):
                            stats = count_x(j + c // U, c % U)
                            if c % NCH == NCH - 1:
                                link(stats)
                                channel_moments(c % U // NCH)
                    ahead = not (last and h == 1)
                    behind = (l - 2) % U
                    if ahead and k == LAST + 3:
                        variance(image + 1)
                    if not (first and l < 2):
                        count_y(j + (l - 2) // U, behind, [0], first)
                    if not (first and l <= LAST):
                        make_lo(h, k, PLACES[l], n)
                    if not (first and l < 2):
                        count_y(j + (l - 2) // U, behind, [1])
                    if ahead and k == LAST + 1:
                        second_moments(image + 1)
                    if ahead and k == LAST + 3:
                        coefficients(image + 1, 1 - h)
                        assert links[1] == PER_IMAGE
                    if k == 1 and not (first and h == 0):
                        image_moments(image - 1, n - 2)

            pair(0, first=True)
            with dve.Fori(1, PAIRS - 1) as j:
                pair(j)
            pair(PAIRS - 1, last=True)
            for l in range(U - 2, U):
                count_y(PAIRS - 1, l, range(CH))
            links[0], links[1] = prologue_links + PER_IMAGE * (B - 1) + 1, 0
            link(image_moments(B - 1, U * PAIRS - 1))

            for ot in range(CT):
                last = v.bn_stats(m_stats[:, ot, :], y_mv[:, ot, :, 0])
            link(last)
            for ot in range(CT):
                v.bn_aggr(m_mv[:, ot, :], m_stats[:, ot, :])
            link(v.tensor_reduce(v_sum[:, :], y_mv[:, :, :, 1], AX_X, ALU.add))
            link(v.scalar_tensor_tensor(b_var[:, :], v_sum[:, :], 1.0 / B, m_mv[:, :, 1], ALU.mult, ALU.add))
            v.tensor_scalar(b_var[:, :], b_var[:, :], w_scale[:, 2:3], None, ALU.add).then_inc(bvar_ready, 1)

            def batch_coefficients():
                dve.wait_ge(bstd_ready, 1)
                newton(b_r[:, :], b_t[:, :], b_var[:, :], b_std[:, :])
                dve.wait_ge(const_in, 48)
                link(v.tensor_tensor(b_r[:, :], b_r[:, :], b_t[:, :], ALU.mult))
                link(v.tensor_tensor(bn_a[:, :], b_r[:, :], gam[:, :], ALU.mult))
                link(v.tensor_tensor(b_t[:, :], m_mv[:, :, 0], bn_a[:, :], ALU.mult))
                link(v.tensor_tensor(bn_b[:, :], bet[:, :], b_t[:, :], ALU.subtract))
                v.tensor_copy(fence[:, :], bn_b[:, 0:1]).then_inc(bn_ready, 1)

            def make_lo2(j, r):
                dve.wait_ge(hi2_ready, NF * j + r + 1)
                v.tensor_tensor(split[:, r % SPLITS, 1, 0:LO_DVE2], g2[:, r % 2, 0:LO_DVE2],
                                split[:, r % SPLITS, 0, 0:LO_DVE2], ALU.subtract).then_inc(lo2_ready, 1)

            def seed2(j, r, row, early):
                n = NF * j + r
                if not early:
                    dve.wait_ge(bn_high_ready, CH * (n - 2) + row + 1)
                dve.wait_ge(both2_done, CH * n + row + 1)
                v.tensor_copy(bank2(r, 2 * row + 1)[:, 0:N], bank2(r, 2 * row)[:, 0:N]).then_inc(seeded2, 1)

            def bn_high(j, r, row, early):
                n, ot = NF * j + r, CH + row
                if row == 0 and not early:
                    wait_r2_free(dve, j, r)
                dve.wait_ge(y2_done, CT * n + 2 * row + 2)
                v.tensor_scalar(r2[:, r % 2, ot, :], bank2(r, 2 * row + 1)[:, 0:N], bn_a[:, ot:ot + 1],
                                bn_b[:, ot:ot + 1], ALU.mult, ALU.add).then_inc(bn_high_ready, 1)

            def add_formed(j, r):
                l, n = FORMED[r], NF * j + r
                xk = xbuf[:, l // NCH, :, cols(l % NCH)]
                dve.wait_ge(bn_low_ready, CH * (n + 1))
                dve.wait_ge(bn_high_ready, CH * (n + 1))
                v.scalar_tensor_tensor(xk, r2[:, r % 2], 0.0, xk, ALU.max, ALU.add).then_inc(sum_ready, 1)

            def add_spilled(j, l):
                h, k, spill = l // NCH, l % NCH, SPILLED.index(l)
                xk = xbuf[:, h, :, cols(k)]
                dve.wait_ge(bn_spill_ready, CT * (NSP * j + spill + 1))
                dve.wait_ge(x_in[h][k], 16 * (PAIRS + j + 1))
                v.scalar_tensor_tensor(xk, y_sb[:, spill % YS], 0.0, xk, ALU.max, ALU.add).then_inc(sum_ready, 1)

            def pair2(j, first=False):
                for l in range(U):
                    if l in SPILLED:
                        continue
                    r = FORMED.index(l)
                    before, r_before = j + (r - 1) // NF, (r - 1) % NF
                    before2, r_before2 = j + (r - 2) // NF, (r - 2) % NF
                    if not (first and r < 2):
                        bn_high(before2, r_before2, 0, first and r < 4)
                    if not (first and r < 1):
                        seed2(before, r_before, 0, first and r < 3)
                    if l - 1 in SPILLED:
                        add_spilled(j, l - 1)
                    make_lo2(j, r)
                    if not (first and r < 2):
                        bn_high(before2, r_before2, 1, first and r < 4)
                    if not (first and r < 1):
                        seed2(before, r_before, 1, first and r < 3)
                    if not (first and r < 2):
                        add_formed(before2, r_before2)
                    if first and r == 0:
                        batch_coefficients()

            pair2(0, first=True)
            with dve.Fori(1, PAIRS) as j:
                pair2(j)
            j = PAIRS - 1
            bn_high(j, NF - 2, 0, False)
            seed2(j, NF - 1, 0, False)
            bn_high(j, NF - 2, 1, False)
            seed2(j, NF - 1, 1, False)
            add_formed(j, NF - 2)
            for row in range(CH):
                bn_high(j, NF - 1, row, False)
            add_formed(j, NF - 1)

        @block.gpsimd
        def _(pool):
            p = nc.gpsimd

            def sum_x(j, l, first):
                n = U * j + l
                pool.wait_ge(g_ready, n + 1)
                if not (first and l < 2):
                    pool.wait_ge(sum_hi_ready, n - 1)
                    pool.wait_ge(sum_lo_ready, n - 1)
                p.tensor_tensor(x_sum[:, l % 2], xbuf[:, l // NCH, 0:CH, cols(l % NCH)],
                                xbuf[:, l // NCH, CH:, cols(l % NCH)], ALU.add).then_inc(x_sum_ready, 1)

            def pair(j, first=False, last=False):
                for l in range(U):
                    h, k, n = l // NCH, l % NCH, U * j + l
                    if not (last and l == U - 1) and not (first and l == 0):
                        sum_x(j + (l + 1) // U, (l + 1) % U, first and l + 1 < U)
                    pool.wait_ge(sum_hi_ready, n + 1)
                    p.tensor_tensor(split[:, PLACES[l], 1, CT:], x_sum[:, l % 2],
                                    split[:, PLACES[l], 0, CT:], ALU.subtract).then_inc(sum_lo_ready, 1)
                    if first and l == 0:
                        sum_x(0, 1, True)
                    pool.wait_ge(hi_ready, n + 1)
                    p.tensor_tensor(split[:, PLACES[l], 1, LO_DVE:CT], xbuf[:, h, LO_DVE:, cols(k)],
                                    split[:, PLACES[l], 0, LO_DVE:CT], ALU.subtract).then_inc(lo1_ready, 1)

            sum_x(0, 0, True)
            pair(0, first=True)
            with pool.Fori(1, PAIRS - 1) as j:
                pair(j)
            pair(PAIRS - 1, last=True)

            def sum_x2(j, r, first):
                n = NF * j + r
                pool.wait_ge(g2_ready, n + 1)
                if not (first and r < 2):
                    pool.wait_ge(sum_hi2_ready, n - 1)
                    pool.wait_ge(sum_lo2_ready, n - 1)
                p.tensor_tensor(x_sum2[:, r % 2], g2[:, r % 2, 0:CH], g2[:, r % 2, CH:],
                                ALU.add).then_inc(x_sum2_ready, 1)

            def bn_spilled(j, spill, ot, first):
                slot = spill % YS
                if first and spill == 0 and ot == 0:
                    pool.wait_ge(bn_ready, 1)
                p.tensor_scalar(y_sb[:, slot, ot, :], y_sb[:, slot, ot, :], bn_a[:, ot:ot + 1],
                                bn_b[:, ot:ot + 1], ALU.mult, ALU.add).then_inc(bn_spill_ready, 1)

            def pair2(j, first=False, last=False):
                for r in range(NF):
                    n = NF * j + r
                    pool.wait_ge(sum_hi2_ready, n + 1)
                    p.tensor_tensor(split[:, r % SPLITS, 1, CT:], x_sum2[:, r % 2], split[:, r % SPLITS, 0, CT:],
                                    ALU.subtract).then_inc(sum_lo2_ready, 1)
                    if not (last and r == NF - 1):
                        sum_x2(j + (r + 1) // NF, (r + 1) % NF, first and r + 1 < NF)
                    for spill, l in enumerate(SPILLED):
                        if r == FORMED.index(l - 1) + 1 - CT:
                            pool.wait_ge(y_back[spill % YS], 16 * (YT * j + spill // YS + 1))
                    pool.wait_ge(hi2_ready, n + 1)
                    p.tensor_tensor(split[:, r % SPLITS, 1, LO_DVE2:CT], g2[:, r % 2, LO_DVE2:],
                                    split[:, r % SPLITS, 0, LO_DVE2:CT], ALU.subtract).then_inc(lo3_ready, 1)
                    for spill, l in enumerate(SPILLED):
                        ot = r - (FORMED.index(l - 1) + 1 - CT)
                        if 0 <= ot < CT:
                            bn_spilled(j, spill, ot, first)

            sum_x2(0, 0, True)
            pair2(0, first=True)
            with pool.Fori(1, PAIRS - 1) as j:
                pair2(j)
            pair2(PAIRS - 1, last=True)

        @block.scalar
        def _(act):
            a = nc.scalar

            def std(image):
                act.wait_ge(var_ready, image + 1)
                a.activation(g_std[:, :], g_var[:, :], ACT.Sqrt).then_inc(std_ready, 1)

            def normalise(j, l):
                h, k = l // NCH, l % NCH
                if k == 0:
                    act.wait_ge(coef_ready, 2 * j + h + 1)
                for ct in range(CT):
                    last = a.activation(xbuf[:, h, ct, cols(k)], xbuf[:, h, ct, cols(k)], ACT.Identity,
                                        bias=coef[:, h, 1, ct:ct + 1], scale=coef[:, h, 0, ct:ct + 1])
                last.then_inc(g_ready, 1)

            def make_sum_hi(j, l, first):
                act.wait_ge(x_sum_ready, U * j + l + 1)
                before = max(c for c in range(-U, l) if PLACES[c] == PLACES[l])
                if before >= 0 or not first:
                    act.wait_ge(y_done, CT * (U * j + before + 1))
                a.copy(split[:, PLACES[l], 0, CT:], x_sum[:, l % 2]).then_inc(sum_hi_ready, 1)

            def make_hi(j, l):
                act.wait_ge(g_ready, U * j + l + 1)
                a.copy(split[:, PLACES[l], 0, 0:CT], xbuf[:, l // NCH, :, cols(l % NCH)]).then_inc(hi_ready, 1)

            def seed(j, l, row, first=False):
                tile = CT * (U * j + l) + 2 * row
                act.wait_ge(both_done, CH * (U * j + l) + row + 1)
                if not (first and CT * l + 2 * row + 1 < NBANK):
                    act.wait_ge(y_counted, tile + 2 - NBANK)
                a.copy(bank(l, 2 * row + 1)[:, 0:N], bank(l, 2 * row)[:, 0:N]).then_inc(seeded, 1)

            std(0)
            normalise(0, 0)
            normalise(0, 1)

            def pair(j, first=False, last=False):
                for l in range(U):
                    if not (first and l < 2):
                        seed(j + (l - 2) // U, (l - 2) % U, 1, first)
                    if not (first and l < 1):
                        seed(j + (l - 1) // U, (l - 1) % U, 0, first)
                    make_sum_hi(j, l, first)
                    make_hi(j, l)
                    if l % NCH == LAST + 3 and not (last and l >= NCH):
                        std(2 * j + l // NCH + 1)
                    if not (last and l >= U - 2):
                        normalise(j + (l + 2) // U, (l + 2) % U)

            pair(0, first=True)
            with act.Fori(1, PAIRS - 1) as j:
                pair(j)
            pair(PAIRS - 1, last=True)
            for l, row in ((U - 2, 1), (U - 1, 0), (U - 1, 1)):
                seed(PAIRS - 1, l, row)

            def fetch_coefficients(image, h):
                a.copy(coef[:, h], coef_all[:, image]).then_inc(coef2_ready, 1)

            def normalise2(j, r, first):
                l, n = FORMED[r], NF * j + r
                h, k = l // NCH, l % NCH
                if r == 0 or FORMED[r - 1] // NCH != h:
                    fetch_coefficients(2 * j + h, h)
                    act.wait_ge(coef2_ready, 2 * j + h + 1)
                if not (first and r < 2):
                    act.wait_ge(lo2_ready, n - 1)
                    act.wait_ge(lo3_ready, n - 1)
                act.wait_ge(x_in[h][k], 16 * (PAIRS + j + 1))
                for ct in range(CT):
                    last = a.activation(g2[:, r % 2, ct, :], xbuf[:, h, ct, cols(k)], ACT.Identity,
                                        bias=coef[:, h, 1, ct:ct + 1], scale=coef[:, h, 0, ct:ct + 1])
                last.then_inc(g2_ready, 1)

            def make_sum_hi2(j, r, first):
                n = NF * j + r
                act.wait_ge(x_sum2_ready, n + 1)
                if not (first and r < SPLITS):
                    act.wait_ge(y2_done, CT * (n - SPLITS + 1))
                a.copy(split[:, r % SPLITS, 0, CT:], x_sum2[:, r % 2]).then_inc(sum_hi2_ready, 1)

            def make_hi2(j, r):
                act.wait_ge(g2_ready, NF * j + r + 1)
                a.copy(split[:, r % SPLITS, 0, 0:CT], g2[:, r % 2]).then_inc(hi2_ready, 1)

            def bn_low(j, r, row, early):
                if row == 0 and not early:
                    wait_r2_free(act, j, r)
                act.wait_ge(y2_done, CT * (NF * j + r) + 2 * row + 1)
                a.activation(r2[:, r % 2, row, :], bank2(r, 2 * row)[:, 0:N], ACT.Identity,
                             bias=bn_b[:, row:row + 1], scale=bn_a[:, row:row + 1]).then_inc(bn_low_ready, 1)

            def pair2(j, first=False, last=False):
                for r in range(NF):
                    before2, r_before2 = j + (r - 2) // NF, (r - 2) % NF
                    make_sum_hi2(j, r, first)
                    if first and r == 2:
                        act.wait_ge(bn_ready, 1)
                    if not (first and r < 2):
                        bn_low(before2, r_before2, 0, first and r < 4)
                    if not (last and r == NF - 1):
                        normalise2(j + (r + 1) // NF, (r + 1) % NF, first and r + 1 < NF)
                    make_hi2(j, r)
                    if not (first and r < 2):
                        bn_low(before2, r_before2, 1, first and r < 4)
                    if first and r == 0:
                        act.wait_ge(bvar_ready, 1)
                        a.activation(b_std[:, :], b_var[:, :], ACT.Sqrt).then_inc(bstd_ready, 1)

            normalise2(0, 0, True)
            act.wait_ge(y_done, CT * U * PAIRS)
            pair2(0, first=True)
            with act.Fori(1, PAIRS - 1) as j:
                pair2(j)
            pair2(PAIRS - 1, last=True)
            for r in range(NF - 2, NF):
                for row in range(CH):
                    bn_low(PAIRS - 1, r, row, False)

        @block.tensor
        def _(pe):
            t = nc.tensor

            def group_means(image):
                pe.wait_ge(mv_ready, image + 1)
                t.matmul(stat_ps[:, 0:CT], gavg[:, :], x_mv[:, :, 0], start=True, stop=True).then_inc(gm_ready, 1)

            def group_variances(image):
                pe.wait_ge(ge_ready, image + 1)
                t.matmul(stat_ps[:, CT:2 * CT], gavg[:, :], g_e[:, :], start=True, stop=True).then_inc(gv_ready, 1)

            def form_half(ps, place, kind, row, add=False):
                if kind == "both":
                    base, w = CT, [(w[:, CH * P:]) for w in (w_hi, w_lo)]
                else:
                    side = int(kind == "high")
                    base, w = side * CH, [w[:, side] for w in (d_hi, d_lo)]
                for c in range(CH):
                    tile = slice((c + row) * P, (c + row + 1) * P)
                    hi, lo = split[:, place, 0, base + c, :], split[:, place, 1, base + c, :]
                    t.matmul(ps, w[0][:, tile], hi, start=(c == 0 and not add), stop=False, skip_group_check=add)
                    t.matmul(ps, w[0][:, tile], lo, start=False, stop=False, skip_group_check=add)
                    last = t.matmul(ps, w[1][:, tile], hi, start=False, stop=(c == CH - 1), skip_group_check=add)
                return last

            def both(j, l, row, first):
                n = U * j + l
                if row == 0:
                    pe.wait_ge(sum_lo_ready, n + 1)
                if not (first and CT * l + 2 * row < NBANK):
                    pe.wait_ge(y_counted, CT * n + 2 * row + 1 - NBANK)
                form_half(bank(l, 2 * row)[:, 0:N], PLACES[l], "both", row).then_inc(both_done, 1)

            def low_and_high(j, l, row):
                n = U * j + l
                if row == 0:
                    pe.wait_ge(lo_ready, n + 1)
                    pe.wait_ge(lo1_ready, n + 1)
                pe.wait_ge(seeded, CH * n + row + 1)
                for i, kind in enumerate(("low", "high")):
                    form_half(bank(l, 2 * row + i)[:, 0:N], PLACES[l], kind, row, add=True).then_inc(y_done, 1)

            def both2(j, r, row, first):
                n = NF * j + r
                if row == 0:
                    pe.wait_ge(sum_lo2_ready, n + 1)
                if not (first and r < 2):
                    pe.wait_ge(bn_low_ready, CH * (n - 2) + row + 1)
                form_half(bank2(r, 2 * row)[:, 0:N], r % SPLITS, "both", row).then_inc(both2_done, 1)

            def low_and_high2(j, r, row):
                n = NF * j + r
                if row == 0:
                    pe.wait_ge(lo2_ready, n + 1)
                    pe.wait_ge(lo3_ready, n + 1)
                pe.wait_ge(seeded2, CH * n + row + 1)
                for i, kind in enumerate(("low", "high")):
                    form_half(bank2(r, 2 * row + i)[:, 0:N], r % SPLITS, kind, row, add=True).then_inc(y2_done, 1)

            pe.wait_ge(const_in, 48)
            group_means(0)
            group_variances(0)
            pe.wait_ge(w_ready, 1)
            for ps in banks:
                t.matmul(ps[:, 0:N], w_hi[:, 0:P], w_hi[:, 0:N], start=True, stop=True)

            def pair(j, first=False, last=False):
                for l in range(U):
                    h, k = l // NCH, l % NCH
                    ahead = not (last and h == 1)
                    for row in range(CH):
                        if row + 1 < CH:
                            both(j, l, row + 1, first)
                        elif not (last and l == U - 1):
                            both(j + (l + 1) // U, (l + 1) % U, 0, first and l + 1 < U)
                        if k == LAST and row == 0 and ahead:
                            group_means(2 * j + h + 1)
                        if k == LAST + 1 and row == 1 and ahead:
                            group_variances(2 * j + h + 1)
                        low_and_high(j, l, row)

            both(0, 0, 0, True)
            pair(0, first=True)
            with pe.Fori(1, PAIRS - 1) as j:
                pair(j)
            pair(PAIRS - 1, last=True)

            pe.wait_ge(y_counted, CT * U * PAIRS)

            def pair2(j, first=False, last=False):
                for r in range(NF):
                    for row in range(CH):
                        if row + 1 < CH:
                            both2(j, r, row + 1, first)
                        elif not (last and r == NF - 1):
                            both2(j + (r + 1) // NF, (r + 1) % NF, 0, first and r + 1 < NF)
                        low_and_high2(j, r, row)

            both2(0, 0, 0, True)
            pair2(0, first=True)
            with pe.Fori(1, PAIRS - 1) as j:
                pair2(j)
            pair2(PAIRS - 1, last=True)


def kernel(x, L0_conv_conv, L0_conv_gamma, L0_conv_beta):
    import concourse.bacc as bacc
    from concourse.bass_utils import run_bass_kernel_spmd

    B, C, H, W = x.shape
    members = C // GROUPS
    group_avg = np.kron(np.eye(P // members), np.full((members, members), 1.0 / members)).astype(np.float32)
    arrays = {
        "x": np.ascontiguousarray(x).reshape(B, C, H * W),
        "conv": np.ascontiguousarray(L0_conv_conv).reshape(-1),
        "gamma": np.ascontiguousarray(L0_conv_gamma),
        "beta": np.ascontiguousarray(L0_conv_beta),
        "group_avg": group_avg,
    }
    nc = bacc.Bacc("TRN2", target_bir_lowering=False, num_devices=1)
    aps = [nc.dram_tensor(n, a.shape, F32, kind="ExternalInput").ap() for n, a in arrays.items()]
    out = nc.dram_tensor("out", (B, C, H * W), F32, kind="ExternalOutput").ap()
    conv_block_kernel(nc, *aps, out)
    r = run_bass_kernel_spmd(nc, [arrays], core_ids=[0])
    return r.results[0]["out"].reshape(B, C, H, W)
```
